# Optimizing a Trainium2 kernel written in Bass

```python
import numpy as np
import jax
import jax.numpy as jnp

def _softmax(x, axis=-1):
    return jax.nn.softmax(x, axis=axis)

def _gelu(x):
    return jax.nn.gelu(x, approximate=True)

def _silu(x):
    return jax.nn.silu(x)

def _sigmoid(x):
    return jax.nn.sigmoid(x)

def _layernorm(x, axis=-1, eps=1e-05):
    m = jnp.mean(x, axis=axis, keepdims=True)
    v = jnp.var(x, axis=axis, keepdims=True)
    return (x - m) / jnp.sqrt(v + eps)

def _scatter_add(tgt, idx, src, axis=0):
    return tgt.at[idx].add(src)

def _segment_sum(src, seg, n):
    return jax.ops.segment_sum(src, seg, n)
kernel_name = 'mk_prb_d1_jaxref_r4_10bb3b'

def setup_inputs(seed: int=0):
    np.random.seed(seed)
    _w = jnp.asarray

    def _L0_attn_setup():
        import jax, jax.numpy as jnp
        import numpy as np
        D_MODEL = 256
        KERNEL_SIZE = 128
        ORDER = 2
        B, T = (4, 512)

        def _layernorm(x, gamma, beta, eps=1e-05):
            mu = jnp.mean(x, axis=-1, keepdims=True)
            var = jnp.mean(jnp.square(x - mu), axis=-1, keepdims=True)
            return (x - mu) * jax.lax.rsqrt(var + eps) * gamma + beta

        def _fft_conv(y_bdt, kernel, T):
            K = kernel.shape[-1]
            kpad = jnp.pad(kernel, ((0, 0), (0, 0), (0, max(0, T - K))))[:, :, :T]
            n = 2 * T
            y_f = jnp.fft.rfft(y_bdt, n=n)
            k_f = jnp.fft.rfft(kpad, n=n)
            conv = jnp.fft.irfft(y_f * k_f, n=n)[:, :, :T]
            return conv
        key = jax.random.key(seed)
        ks = jax.random.split(key, 8)
        x = jax.random.normal(ks[0], (B, T, D_MODEL), dtype=jnp.float32)
        W_in = jax.random.normal(ks[1], (D_MODEL, D_MODEL * (ORDER + 1)), dtype=jnp.float32) * (1.0 / np.sqrt(D_MODEL))
        b_in = jnp.zeros((D_MODEL * (ORDER + 1),), dtype=jnp.float32)
        k0 = jax.random.normal(ks[2], (1, D_MODEL, KERNEL_SIZE), dtype=jnp.float32) * 0.02
        k1 = jax.random.normal(ks[3], (1, D_MODEL, KERNEL_SIZE), dtype=jnp.float32) * 0.02
        gamma = jnp.ones((D_MODEL,), dtype=jnp.float32)
        beta = jnp.zeros((D_MODEL,), dtype=jnp.float32)
        W_out = jax.random.normal(ks[4], (D_MODEL, D_MODEL), dtype=jnp.float32) * (1.0 / np.sqrt(D_MODEL))
        b_out = jnp.zeros((D_MODEL,), dtype=jnp.float32)
        return {'x': x, 'W_in': W_in, 'b_in': b_in, 'k0': k0, 'k1': k1, 'gamma': gamma, 'beta': beta, 'W_out': W_out, 'b_out': b_out}
    _L0_attn_in = _L0_attn_setup()

    def _L0_ffn_setup():
        import jax, jax.numpy as jnp
        import numpy as np
        DIM = 256
        HIDDEN = 768
        SCALE = 1.0 / 127.0

        def _dequant(w_int, dtype):
            return w_int.astype(dtype) * jnp.asarray(SCALE, dtype)
        key = jax.random.key(seed)
        k_x, k_g, k_u, k_d = jax.random.split(key, 4)
        x = jax.random.normal(k_x, (4, 512, DIM), dtype=jnp.float32)
        w_gate = jax.random.randint(k_g, (HIDDEN, DIM), -127, 128, dtype=jnp.int32)
        w_up = jax.random.randint(k_u, (HIDDEN, DIM), -127, 128, dtype=jnp.int32)
        w_down = jax.random.randint(k_d, (DIM, HIDDEN), -127, 128, dtype=jnp.int32)
        return {'x': x, 'w_gate': w_gate, 'w_up': w_up, 'w_down': w_down}
    _L0_ffn_in = _L0_ffn_setup()
    _d = {'L0_attn_x': _L0_attn_in['x'], 'L0_attn_W_in': _L0_attn_in['W_in'], 'L0_attn_b_in': _L0_attn_in['b_in'], 'L0_attn_k0': _L0_attn_in['k0'], 'L0_attn_k1': _L0_attn_in['k1'], 'L0_attn_gamma': _L0_attn_in['gamma'], 'L0_attn_beta': _L0_attn_in['beta'], 'L0_attn_W_out': _L0_attn_in['W_out'], 'L0_attn_b_out': _L0_attn_in['b_out'], 'L0_ffn_w_gate': _L0_ffn_in['w_gate'], 'L0_ffn_w_up': _L0_ffn_in['w_up'], 'L0_ffn_w_down': _L0_ffn_in['w_down']}
    _x0 = _d['L0_attn_x']
    _d['L0_attn_x'] = jax.random.normal(jax.random.fold_in(jax.random.key(seed), 1), (1, 4096, 256), dtype=_x0.dtype)
    del _x0
    return _d

def reference(L0_attn_x, L0_attn_W_in, L0_attn_b_in, L0_attn_k0, L0_attn_k1, L0_attn_gamma, L0_attn_beta, L0_attn_W_out, L0_attn_b_out, L0_ffn_w_gate, L0_ffn_w_up, L0_ffn_w_down):

    def _L0_attn_ref(x, W_in, b_in, k0, k1, gamma, beta, W_out, b_out):
        import jax, jax.numpy as jnp
        import numpy as np
        D_MODEL = 256
        KERNEL_SIZE = 128
        ORDER = 2
        B, T = (4, 512)

        def _layernorm(x, gamma, beta, eps=1e-05):
            mu = jnp.mean(x, axis=-1, keepdims=True)
            var = jnp.mean(jnp.square(x - mu), axis=-1, keepdims=True)
            return (x - mu) * jax.lax.rsqrt(var + eps) * gamma + beta

        def _fft_conv(y_bdt, kernel, T):
            K = kernel.shape[-1]
            kpad = jnp.pad(kernel, ((0, 0), (0, 0), (0, max(0, T - K))))[:, :, :T]
            n = 2 * T
            y_f = jnp.fft.rfft(y_bdt, n=n)
            k_f = jnp.fft.rfft(kpad, n=n)
            conv = jnp.fft.irfft(y_f * k_f, n=n)[:, :, :T]
            return conv
        Bn, Tn, Dn = x.shape
        residual = x
        xn = _layernorm(x, gamma, beta)
        proj = (xn @ W_in + b_in).reshape(Bn, Tn, ORDER + 1, Dn)
        v = proj[:, :, 0, :]
        y = jnp.transpose(v, (0, 2, 1))
        for i, kern in enumerate((k0, k1)):
            xi = jnp.transpose(proj[:, :, i + 1, :], (0, 2, 1))
            y = _fft_conv(y, kern, Tn) * xi
        y = jnp.transpose(y, (0, 2, 1))
        y = y @ W_out + b_out
        return residual + y

    def _L0_ffn_ref(x, w_gate, w_up, w_down):
        import jax, jax.numpy as jnp
        import numpy as np
        DIM = 256
        HIDDEN = 768
        SCALE = 1.0 / 127.0

        def _dequant(w_int, dtype):
            return w_int.astype(dtype) * jnp.asarray(SCALE, dtype)
        wg = _dequant(w_gate, x.dtype)
        wu = _dequant(w_up, x.dtype)
        wd = _dequant(w_down, x.dtype)
        gate = jnp.einsum('bsd,hd->bsh', x, wg)
        up = jnp.einsum('bsd,hd->bsh', x, wu)
        h = jax.nn.silu(gate) * up
        return jnp.einsum('bsh,dh->bsd', h, wd)
    x = L0_attn_x
    xn = _layernorm(x, axis=-1)
    x = x + _L0_attn_ref(xn, L0_attn_W_in, L0_attn_b_in, L0_attn_k0, L0_attn_k1, L0_attn_gamma, L0_attn_beta, L0_attn_W_out, L0_attn_b_out) + _L0_ffn_ref(xn, L0_ffn_w_gate, L0_ffn_w_up, L0_ffn_w_down)
    return x

_drawn_inputs = setup_inputs


def setup_inputs(seed=0):
    import zlib

    import numpy as np

    out = dict(_drawn_inputs(seed))
    spreads = {'L0_attn_b_in': (0.0, 0.8),
     'L0_attn_gamma': (1.0, 0.6),
     'L0_attn_beta': (0.0, 0.8),
     'L0_attn_b_out': (0.0, 0.8)}
    factors = {'L0_attn_W_in': 8.0, 'L0_attn_k0': 8.0, 'L0_attn_k1': 8.0, 'L0_attn_W_out': 8.0}
    for name, (base, spread) in spreads.items():
        noise = np.random.default_rng([zlib.crc32(name.encode()), seed]).standard_normal(out[name].shape)
        drawn = base * np.exp(spread * noise) if base else spread * noise
        out[name] = jnp.asarray(drawn.astype(out[name].dtype))
    for name, factor in factors.items():
        out[name] = (out[name] * factor).astype(out[name].dtype)
    return out
```

```python
from contextlib import ExitStack

import concourse.bass as bass
from concourse import mybir

P = 128
ALU = mybir.AluOpType
ACT = mybir.ActivationFunctionType
F32 = mybir.dt.float32
F16 = mybir.dt.float16
I32 = mybir.dt.int32
U32 = mybir.dt.uint32
AX = mybir.AxisListType


def hyena_ffn_kernel(nc, x, W_in, b_in, k0, k1, gamma, beta, W_out, b_out, w_gate, w_up, w_down, out):
    T, D = x.shape[1], x.shape[2]
    K = k0.shape[2]
    H = w_gate.shape[0]
    NB = T // P
    KD = D // P
    HB = H // P
    NQ = 4
    CQ = D // NQ
    CG = 16
    GQ = CQ // CG
    NG = NQ * GQ
    CHUNK = 512
    NCHUNK = T // CHUNK
    TPC = CHUNK // P
    STEPS = NCHUNK * HB
    SQ = STEPS // NQ
    SG = SQ // GQ
    BATCH = 8
    NBATCH = NB // BATCH
    SPLIT = 4
    NSPLIT = NB // SPLIT
    ROWS = 16
    STRIP = K + ROWS
    PADW = ROWS + K + ROWS
    EPS = 1e-5
    TINY = 1e-30
    EXPONENT = 0x7F800000
    XN_MAX = 16.0
    TOP = 2.0 ** 15
    KTOP = 2.0 ** 8
    Y1_SCALE = 1.0 / (TOP * K * KTOP)
    assert K == P and NB * CG == 512 and SQ % 6 == 0 and HB == 6 and SG == 3 and XN_MAX ** 2 >= D

    x_v = x.rearrange("o (b p) d -> p (o b) d", p=P)
    out_v = out.rearrange("o (b p) d -> p (o b) d", p=P)
    shifted = nc.dram_tensor("shifted_kernels", [ROWS, 2, D, STRIP, 2], F16, kind="Internal").ap()

    with ExitStack() as ctx:
        def sb(name, shape, dt=F32):
            return ctx.enter_context(nc.sbuf_tensor(name, shape, dt))

        def sem(name):
            return ctx.enter_context(nc.semaphore(name))

        def bank(name):
            return ctx.enter_context(nc.psum_tensor(name, [P, 512], F32))

        res = sb("res", [P, NB, D])
        xT = sb("xT", [P, 4, T], F16)
        y2 = sb("y2", [P, D, NB])
        vx = sb("vx", [P, 3, CQ, NB])
        vhl = sb("vhl", [P, 2, CQ, NB], F16)
        wq = sb("wq", [P, 2, KD, 3 * D], F16)
        wgu = sb("wgu", [P, 2, KD, 2 * H], F16)
        wd = sb("wd", [P, 2, HB, D], F16)
        wo = sb("wo", [P, 2, KD, D], F16)
        bands = sb("bands", [P, 2, CG, 2 * P, 2], F16)
        sgh = sb("sgh", [P, 2, CHUNK])
        hhl = sb("hhl", [P, 3, 2, CHUNK], F16)
        y1f = sb("y1f", [P, CG, NB])
        y1hl = sb("y1hl", [P, 2, CG, NB], F16)
        bias = sb("bias", [P, 3 * D])
        bout = sb("bout", [P, D])
        ident = sb("ident", [P, P], F16)
        stats = sb("stats", [P, BATCH, 6])
        mv = sb("mv", [P, NB, 2])
        lns = sb("lns", [P, 6, NB])
        minus_half = sb("minus_half", [P, BATCH])
        gb = sb("gb", [P, 2, KD])
        kmax = sb("kmax", [P, 2, KD, 2])
        sdg = sb("sdg", [P, 6])
        qch = sb("qch", [P, KD])
        cst = sb("cst", [P, 24])
        flag = sb("flag", [P, 1], I32)
        ymax = sb("ymax", [P, NG, NB])
        st = lns[:, 3:6, :]

        r1, r2, r1p, nmr, ls0, ls1 = (lns[:, i, :] for i in range(6))
        xn = sgh[:, :, :].rearrange("p a (b d) -> p (a b) d", d=D)
        xhl = hhl[:, 0:2, :, :].rearrange("p a h (b d) -> p (a h b) d", d=D)
        y2flat = y2[:, :, :].rearrange("p c b -> p (c b)")
        vxflat = vx[:, :, :, :].rearrange("p i c b -> p (i c b)")
        at = [0, 0]

        def part(which, n):
            flat = (y2flat, vxflat)[which]
            at[which] += n
            return flat[:, at[which] - n:at[which]]

        gu_int = part(0, 2 * HB * D).bitcast(I32).rearrange("p (u d) -> p u d", d=D)
        wd_int = part(0, KD * H).bitcast(I32).rearrange("p (a h) -> p a h", a=KD)
        win = part(0, KD * 3 * D).rearrange("p (k n) -> p k n", k=KD)
        wsq = part(1, KD * 3 * D).rearrange("p (k n) -> p k n", k=KD)
        wout = part(0, KD * D).rearrange("p (k n) -> p k n", k=KD)
        wgm = part(1, KD * 3 * D).rearrange("p (k n) -> p k n", k=KD)
        scl = part(1, 3 * D)
        nrm = part(1, 3 * D)
        kin = part(0, KD * 2 * K).rearrange("p (h v t) -> p h v t", h=KD, v=2)
        kpd = part(0, KD * 2 * PADW).bitcast(F16).rearrange("p (h v w e) -> p h v w e", h=KD, v=2, e=2)
        ident32 = part(1, P)
        bbc = part(1, KD * P).rearrange("p (k n) -> p k n", k=KD)
        ones = part(1, P)
        bin_row = part(1, 3 * D)
        dg = y1f[:, :, :].rearrange("p c b -> p (c b)")
        units = [*(y1hl[:, i, :, :].rearrange("p c b -> p (c b)").rearrange("p (e d) -> p e d", e=2) for i in range(2)),
                 *(dg[:, i * D:(i + 1) * D].bitcast(F16).rearrange("p (e d) -> p e d", e=2) for i in range(2))]
        ysc = vxflat[:, 0:4 * D].rearrange("p (r d) -> p r d", d=D)
        yhl = vxflat[:, 4 * D:8 * D].bitcast(F16).rearrange("p (r e d) -> p r e d", r=4, e=2)
        yT = vxflat[:, 8 * D:10 * D].bitcast(F16).rearrange("p (r i t) -> p r i t", r=2, i=4)

        bank_g = [bank(f"bank_g{i}") for i in range(2)]
        bank_u = [bank(f"bank_u{i}") for i in range(2)]
        bank_d = [bank(f"bank_d{i}") for i in range(2)]
        bank_c = [bank(f"bank_c{i}") for i in range(2)]

        x_loaded = [sem(f"x_loaded{i}") for i in range(NBATCH)]
        win_loaded, gb_loaded, bin_loaded, bout_loaded = sem("win_loaded"), sem("gb_loaded"), sem("bin_loaded"), sem("bout_loaded")
        k_loaded, wout_loaded, int_loaded = sem("k_loaded"), sem("wout_loaded"), sem("int_loaded")
        consts_ready = sem("consts_ready")
        bands_zeroed = sem("bands_zeroed")
        dve_chain, act_chain, pool_chain = sem("dve_chain"), sem("act_chain"), sem("pool_chain")
        wsq_ready = sem("wsq_ready")
        norm_mm, norm_ready = sem("norm_mm"), sem("norm_ready")
        wgm_ready, wqh_ready, wql_ready = sem("wgm_ready"), sem("wqh_ready"), sem("wql_ready")
        kpad_ready, kpad_stored = sem("kpad_ready"), sem("kpad_stored")
        part_max, all_max = sem("part_max"), sem("all_max")
        wo_ready, ffn_consts = sem("wo_ready"), sem("ffn_consts")
        unit_h, unit_l, unit_tp, unit_ev = sem("unit_h"), sem("unit_l"), sem("unit_tp"), sem("unit_ev")
        flag_ready = sem("flag_ready")
        stats_ready, r_ready = sem("stats_ready"), sem("r_ready")
        xn_ready, xh_ready, xl_ready, res_ready, bout_added = (
            sem("xn_ready"), sem("xh_ready"), sem("xl_ready"), sem("res_ready"), sem("bout_added"))
        xT_tp, xT_ev = sem("xT_tp"), sem("xT_ev")
        proj_mm, proj_ev = sem("proj_mm"), sem("proj_ev")
        vh_ready, vl_ready = sem("vh_ready"), sem("vl_ready")
        band_loaded = [sem(f"band_loaded{i}") for i in range(2)]
        conv_mm = sem("conv_mm")
        y1_ready, y1h_ready, y1l_ready, y2_ready, ymax_ready = (
            sem("y1_ready"), sem("y1h_ready"), sem("y1l_ready"), sem("y2_ready"), sem("ymax_ready"))
        gu_mm, sg_ready, h_ready, hh_ready, hl_ready, down_mm, folded = (
            sem("gu_mm"), sem("sg_ready"), sem("h_ready"), sem("hh_ready"), sem("hl_ready"), sem("down_mm"), sem("folded"))
        ysc_ready, yh_ready, yl_ready, yT_tp, yT_ev, out_mm, out_ready = (
            sem("ysc_ready"), sem("yh_ready"), sem("yl_ready"), sem("yT_tp"), sem("yT_ev"), sem("out_mm"), sem("out_ready"))
        out_stored = sem("out_stored")

        def c(i, n=1):
            return cst[:, i:i + n]

        C_PMAX, C_MAX, C_REC, C_POW, C_SC = 0, 3, 6, 9, 12
        C_GS, C_HS, C_FS = 15, 16, 17
        C_OP, C_OM, C_OS, C_T, C_T2, C_LP = 18, 19, 20, 21, 22, 23

        def bcast(ap, n):
            return bass.AP(ap.tensor, ap.offset, [ap.ap[0], [0, n], ap.ap[1]])

        def col(ap, i):
            return ap[:, i:i + 1]

        block = ctx.enter_context(nc.Block())

        @block.sync
        def _(sp):
            for m in range(NBATCH):
                sp.dma_start(res[:, m * BATCH:(m + 1) * BATCH, :], x_v[:, m * BATCH:(m + 1) * BATCH, :]).then_inc(x_loaded[m], 16)
                if m == 0:
                    for h in range(KD):
                        sp.dma_start(kin[:, h, 0, :], k0[0, h * P:(h + 1) * P, :]).then_inc(k_loaded, 16)
                        sp.dma_start(kin[:, h, 1, :], k1[0, h * P:(h + 1) * P, :]).then_inc(k_loaded, 16)
            sp.wait_ge(kpad_ready, 2)
            for i in range(ROWS):
                for h in range(KD):
                    sp.dma_start(shifted[i, :, h * P:(h + 1) * P, :, :].rearrange("v p w e -> p v (w e)"),
                                 kpd[:, h, :, ROWS - i:ROWS - i + STRIP, :].rearrange("p v w e -> p v (w e)")).then_inc(kpad_stored, 16)
            sp.wait_ge(kpad_stored, 16 * ROWS * KD)
            sp.wait_ge(bands_zeroed, 1)

            def load_bands(G, v, first):
                if not first:
                    sp.wait_ge(conv_mm, 2 * (G - 1) + v + 1)
                src = shifted[:, v, bass.ds(G * CG, CG), :, :].rearrange("i c w e -> i c (w e)")
                for r in range(P // ROWS):
                    dst = bands[r * ROWS:(r + 1) * ROWS, v, :, r * ROWS:r * ROWS + STRIP, :].rearrange("p c w e -> p c (w e)")
                    sp.dma_start(dst, src).then_inc(band_loaded[v], 16)

            for v in range(2):
                load_bands(0, v, True)
            with sp.Fori(1, NG) as G:
                for v in range(2):
                    load_bands(G, v, False)

            SB = 4

            def store(i):
                sp.wait_ge(out_ready, SB * i + SB)
                sp.dma_start(out_v[:, bass.ds(SB * i, SB), :], res[:, bass.ds(SB * i, SB), :]).then_inc(out_stored, 16)

            with sp.Fori(0, NB // SB) as i:
                store(i)
            sp.wait_ge(out_stored, 16 * (NB // SB))

        @block.tensor
        def _(pe):
            def mm(o, w, m, start, stop):
                return nc.tensor.matmul(o, w, m, start=start, stop=stop, skip_group_check=True)

            pe.wait_ge(wsq_ready, 1)
            half = 3 * D // 2
            for i in range(2):
                cols = slice(i * half, (i + 1) * half)
                for dst, lhs, rhs in ((bank_d[i], lambda k: ones, wsq), (bank_u[i], lambda k: bbc[:, k, :], win)):
                    for k in range(KD):
                        last = mm(dst[:, 0:half], lhs(k), rhs[:, k, cols], k == 0, k == KD - 1)
            last.then_inc(norm_mm, 1)

            def transpose_x(b):
                pe.wait_ge(xh_ready, b + 1)
                pe.wait_ge(xl_ready, b + 1)
                if b >= 2:
                    pe.wait_ge(xT_ev, b - 1)
                o = bank_g[b % 2].bitcast(F16)
                for e in range(2):
                    for k in range(KD):
                        i = 2 * e + k
                        last = nc.tensor.transpose(o[:, i * P:(i + 1) * P], xhl[:, 2 * (b % 4) + e, k * P:(k + 1) * P], ident[:, :])
                last.then_inc(xT_tp, 1)

            def project(q, b, par, first, clear=None):
                if not (first and par == b):
                    pe.wait_ge(proj_ev, NB * q + b - 1)
                if clear is not None:
                    pe.wait_ge(*clear)
                o = bank_c[par][:, 0:3 * CQ]
                n = 0
                for e, f in ((0, 0), (1, 0), (0, 1)):
                    for k in range(KD):
                        last = mm(o, xT[:, 2 * e + k, bass.ds(b * P, P)], wq[:, f, k, bass.ds(q * 3 * CQ, 3 * CQ)], n == 0, n == 5)
                        n += 1
                last.then_inc(proj_mm, 1)

            pe.wait_ge(consts_ready, 1)
            LAG = 2
            for b in range(NB + LAG):
                if b < NB:
                    transpose_x(b)
                if b >= LAG:
                    if b == LAG:
                        pe.wait_ge(wqh_ready, 2)
                        pe.wait_ge(wql_ready, 2)
                    pe.wait_ge(xT_ev, b - LAG + 1)
                    project(0, b - LAG, (b - LAG) % 2, b - LAG < 2)

            for u in range(3 * HB):
                pe.wait_ge(unit_h, u + 1)
                pe.wait_ge(unit_l, u + 1)
                if u >= 2:
                    pe.wait_ge(unit_ev, u - 1)
                o = bank_u[u % 2].bitcast(F16)
                for e in range(2):
                    for k in range(2):
                        i = 2 * e + k
                        last = nc.tensor.transpose(o[:, i * P:(i + 1) * P], units[u % 4][:, e, k * P:(k + 1) * P], ident[:, :])
                last.then_inc(unit_tp, 1)

            def gate_up(q, j, first, general):
                n, h = SQ * q + j, j % HB
                if not (first and j < 2):
                    pe.wait_ge(h_ready, n - 1)
                tok = bass.ds((2 * q + j // HB) * CHUNK, CHUNK)
                for o, u in ((bank_g[j % 2], h), (bank_u[j % 2], HB + h)):
                    terms = [(0, 0), (1, 0)] + ([(0, 1)] if general else [])
                    i = 0
                    for e, f in terms:
                        for k in range(KD):
                            last = mm(o[:, :], wgu[:, f, k, u * P:(u + 1) * P], xT[:, 2 * e + k, tok], i == 0, i == KD * len(terms) - 1)
                            i += 1
                last.then_inc(gu_mm, 1)

            def down(q, j, first, general):
                n, h = SQ * q + j, j % HB
                pe.wait_ge(hh_ready, n + 1)
                pe.wait_ge(hl_ready, n + 1)
                if h == 0 and not (first and j < HB):
                    pe.wait_ge(folded, 2 * (2 * q + j // HB))
                for t in range(TPC):
                    o = bank_d[t // 2][:, (t % 2) * D:(t % 2 + 1) * D]
                    tok = slice(t * P, (t + 1) * P)
                    ring = hhl[:, j % 3]
                    terms = [(0, 0), (1, 0)] + ([(0, 1)] if general else [])
                    for i, (e, f) in enumerate(terms):
                        last = mm(o, ring[:, e, tok], wd[:, f, h, :], h == 0 and i == 0 and t % 2 == 0,
                                  h == HB - 1 and i == len(terms) - 1)
                last.then_inc(down_mm, 1)

            def convolve(q, g, v, first):
                G = GQ * q + g
                pe.wait_ge(band_loaded[v], 16 * (P // ROWS) * (G + 1))
                if v == 0:
                    if g == 0:
                        pe.wait_ge(vl_ready, NSPLIT * (q + 1))
                        pe.wait_ge(vh_ready, NSPLIT * (q + 1))
                    src = [vhl[:, e, g * CG:(g + 1) * CG, :] for e in range(2)]
                    if not (first and g == 0):
                        pe.wait_ge(y1_ready, G)
                else:
                    pe.wait_ge(y1h_ready, G + 1)
                    pe.wait_ge(y1l_ready, G + 1)
                    src = [y1hl[:, e, :, :] for e in range(2)]
                    if not (first and g == 0):
                        pe.wait_ge(y2_ready, G)
                if g == 0:
                    pe.wait_ge(proj_ev, NB * (q + 1))
                for i in range(CG):
                    o = bank_c[v][:, i * NB:(i + 1) * NB]
                    T0 = [bands[:, v, i, 0:P, f] for f in range(2)]
                    T1 = [bands[:, v, i, P:2 * P, f] for f in range(2)]
                    hi, lo = (s[:, i, :] for s in src)
                    mm(o, T0[0], hi, True, False)
                    mm(o, T0[0], lo, False, False)
                    mm(o[:, 1:NB], T1[0], hi[:, 0:NB - 1], False, False)
                    mm(o[:, 1:NB], T1[0], lo[:, 0:NB - 1], False, False)
                    mm(o[:, 1:NB], T1[1], hi[:, 0:NB - 1], False, False)
                    last = mm(o, T0[1], hi, False, True)
                last.then_inc(conv_mm, 1)

            def ffn_step(q, j, first, general):
                gate_up(q, j, first, general)
                if not (first and j < 2):
                    down(q - 1 if j < 2 else q, (j - 2) % SQ, first, general)

            def quarter(q, first, general):
                if not first:
                    project(q, 0, 0, False, (y1_ready, GQ * q))
                    project(q, 1, 1, False, (y2_ready, GQ * q))
                    with pe.Fori(1, NB // 2) as i:
                        project(q, 2 * i, 0, False)
                        project(q, 2 * i + 1, 1, False)
                for g in range(GQ):
                    ffn_step(q, SG * g, first, general)
                    convolve(q, g, 0, first)
                    ffn_step(q, SG * g + 1, first, general)
                    ffn_step(q, SG * g + 2, first, general)
                    convolve(q, g, 1, first)

            def body(general):
                quarter(0, True, general)
                with pe.Fori(1, NQ) as q:
                    quarter(q, False, general)
                for j in (SQ - 2, SQ - 1):
                    down(NQ - 1, j, False, general)

            pe.wait_ge(unit_ev, 3 * HB)
            pe.wait_ge(flag_ready, 1)
            general = pe.value_load(flag[0:1, 0:1], min_val=0, max_val=1)
            with pe.If(general > 0):
                body(True)
            with pe.Else():
                body(False)

            def transpose_y(b, par, first):
                pe.wait_ge(yh_ready, b + 1)
                pe.wait_ge(yl_ready, b + 1)
                if not first:
                    pe.wait_ge(yT_ev, b - 1)
                o = bank_g[par % 2].bitcast(F16)
                for e in range(2):
                    for k in range(KD):
                        i = 2 * e + k
                        last = nc.tensor.transpose(o[:, i * P:(i + 1) * P], yhl[:, par, e, k * P:(k + 1) * P], ident[:, :])
                last.then_inc(yT_tp, 1)

            def project_out(b, par, first):
                pe.wait_ge(yT_ev, b + 1)
                if not first:
                    pe.wait_ge(out_ready, b - 1)
                n = 0
                for e, f in ((0, 0), (1, 0), (0, 1)):
                    for k in range(KD):
                        last = mm(bank_c[par][:, 0:D], yT[:, par, 2 * e + k, :], wo[:, f, k, :], n == 0, n == 5)
                        n += 1
                last.then_inc(out_mm, 1)

            pe.wait_ge(wo_ready, 2)
            pe.wait_ge(h_ready, STEPS)
            pe.wait_ge(y2_ready, NG)
            transpose_y(0, 0, True)
            transpose_y(1, 1, True)
            project_out(0, 0, True)
            transpose_y(2, 2, False)
            project_out(1, 1, True)
            transpose_y(3, 3, False)
            project_out(2, 0, False)
            with pe.Fori(1, NB // 4) as i:
                for r in range(4):
                    transpose_y(4 * i + r, r, False)
                    project_out(4 * i + r - 1, (r - 1) % 2, False)
            project_out(NB - 1, 1, False)

        @block.scalar
        def _(act):
            for dst, src, s in (
                *((gb[:, i, k:k + 1], a[k * P:(k + 1) * P].rearrange("(p o) -> p o", o=1), gb_loaded)
                  for i, a in enumerate((gamma, beta)) for k in range(KD)),
                (win[:, :, :], W_in.rearrange("(k p) n -> p k n", p=P), win_loaded),
                (bin_row[:, :], bass.AP(b_in.tensor, b_in.offset, [[0, P], [1, 3 * D]]), bin_loaded),
                (wout[:, :, :], W_out.rearrange("(k p) n -> p k n", p=P), wout_loaded),
                (bout[:, :], bass.AP(b_out.tensor, b_out.offset, [[0, P], [1, D]]), bout_loaded),
                (gu_int[:, 0:HB, :], w_gate.rearrange("(u p) d -> p u d", p=P), int_loaded),
                (gu_int[:, HB:2 * HB, :], w_up.rearrange("(u p) d -> p u d", p=P), int_loaded),
                (wd_int[:, :, :], w_down.rearrange("(a p) h -> p a h", p=P), int_loaded),
            ):
                act.dma_start(dst, src).then_inc(s, 16)

            half = 3 * D // 2
            act.wait_ge(norm_mm, 1)
            for i in range(2):
                nc.scalar.activation(nrm[:, i * half:(i + 1) * half], bank_d[i][:, 0:half], ACT.Sqrt,
                                     scale=XN_MAX * XN_MAX).then_inc(norm_ready, 1)

            def round_x(b):
                act.wait_ge(xn_ready, b + 1)
                if b >= 4:
                    act.wait_ge(xT_tp, b - 3)
                nc.scalar.copy(xhl[:, 2 * (b % 4), :], xn[:, b % 4, :]).then_inc(xh_ready, 1)

            def evacuate_x(b):
                act.wait_ge(xT_tp, b + 1)
                nc.scalar.copy(xT[:, :, b * P:(b + 1) * P],
                               bank_g[b % 2].bitcast(F16)[:, 0:512].rearrange("p (i t) -> p i t", i=4)).then_inc(xT_ev, 1)

            def split_v(q, m):
                nc.scalar.copy(vhl[:, 0, :, bass.ds(SPLIT * m, SPLIT)], vx[:, 0, :, bass.ds(SPLIT * m, SPLIT)]).then_inc(vh_ready, 1)

            round_x(0)
            round_x(1)
            act.wait_ge(wgm_ready, 2)
            for k in range(KD):
                nc.scalar.copy(wq[:, 0, k, :].rearrange("p (q i c) -> p i q c", q=NQ, i=3),
                               wgm[:, k, :].rearrange("p (i q c) -> p i q c", q=NQ, i=3)).then_inc(wqh_ready, 1)
            for b in range(NB + 6):
                if 2 <= b < NB:
                    round_x(b)
                if 1 <= b <= NB:
                    evacuate_x(b - 1)
                if b >= 6 and (b - 6) % SPLIT == SPLIT - 1:
                    act.wait_ge(proj_ev, b - 6 + 1)
                    split_v(0, (b - 6) // SPLIT)

            act.wait_ge(ffn_consts, 1)

            def unit(u):
                if u < 2 * HB:
                    return gu_int[:, u, :], c(C_SC + u // HB)
                return wd_int[:, (u - 2 * HB) // 3, ((u - 2 * HB) % 3) * D:((u - 2 * HB) % 3 + 1) * D], c(C_SC + 2)

            for u in range(3 * HB + 2):
                if u < 3 * HB:
                    src, s = unit(u)
                    if u >= 4:
                        act.wait_ge(unit_tp, u - 3)
                    nc.scalar.activation(units[u % 4][:, 0, :], src, ACT.Copy, scale=s).then_inc(unit_h, 1)
                if u >= 2:
                    w = u - 2
                    act.wait_ge(unit_tp, w + 1)
                    o = bank_u[w % 2].bitcast(F16)[:, 0:512].rearrange("p (e k t) -> p e k t", e=2, k=2)
                    if w < 2 * HB:
                        dst = wgu[:, :, :, w * P:(w + 1) * P]
                    else:
                        a, jj = divmod(w - 2 * HB, 3)
                        dst = wd[:, :, 2 * jj:2 * jj + 2, a * P:(a + 1) * P]
                    nc.scalar.copy(dst, o).then_inc(unit_ev, 1)

            def silu(q, j, first):
                n = SQ * q + j
                act.wait_ge(gu_mm, n + 1)
                if not (first and j < 2):
                    act.wait_ge(hl_ready, n - 1)
                nc.scalar.activation(sgh[:, j % 2, :], bank_g[j % 2][:, :], ACT.Silu, scale=c(C_GS)).then_inc(sg_ready, 1)

            def round_h(q, j, first):
                n = SQ * q + j
                act.wait_ge(h_ready, n + 1)
                if not (first and j < 3):
                    act.wait_ge(down_mm, n - 2)
                nc.scalar.copy(hhl[:, j % 3, 0, :], sgh[:, j % 2, :]).then_inc(hh_ready, 1)

            def ffn_step(q, j, first):
                silu(q, j, first)
                if not (first and j < 1):
                    round_h(q - 1 if j < 1 else q, (j - 1) % SQ, first)

            def round_y1(q, g, first):
                G = GQ * q + g
                act.wait_ge(y1_ready, G + 1)
                if not (first and g == 0):
                    act.wait_ge(conv_mm, 2 * G)
                nc.scalar.copy(y1hl[:, 0, :, :], y1f[:, :, :]).then_inc(y1h_ready, 1)

            def quarter(q, first):
                if not first:
                    act.wait_ge(conv_mm, 2 * GQ * q - 1)
                    with act.Fori(0, NSPLIT) as m:
                        act.wait_ge(proj_ev, NB * q + SPLIT * m + SPLIT)
                        split_v(q, m)
                for g in range(GQ):
                    ffn_step(q, SG * g, first)
                    round_y1(q, g, first)
                    ffn_step(q, SG * g + 1, first)
                    ffn_step(q, SG * g + 2, first)

            quarter(0, True)
            with act.Fori(1, NQ) as q:
                quarter(q, False)
            round_h(NQ - 1, SQ - 1, False)

            def round_y(b, r, first):
                act.wait_ge(ysc_ready, b + 1)
                if not first:
                    act.wait_ge(yT_tp, b - 3)
                nc.scalar.copy(yhl[:, r, 0, :], ysc[:, r, :]).then_inc(yh_ready, 1)

            def evacuate_y(b, r, first):
                act.wait_ge(yT_tp, b + 1)
                if not first:
                    act.wait_ge(out_mm, b - 1)
                nc.scalar.copy(yT[:, r % 2, :, :], bank_g[r % 2].bitcast(F16)[:, 0:512].rearrange("p (i t) -> p i t", i=4)).then_inc(yT_ev, 1)

            for r in range(4):
                round_y(r, r, True)
                if r >= 1:
                    evacuate_y(r - 1, r - 1, r - 1 < 2)
            with act.Fori(1, NB // 4) as i:
                for r in range(4):
                    round_y(4 * i + r, r, False)
                    evacuate_y(4 * i + r - 1, (r - 1) % 4, False)
            evacuate_y(NB - 1, 3, False)

        @block.vector
        def _(dve):
            chain = [0]

            def link(ins):
                chain[0] += 1
                ins.then_inc(dve_chain, 1)
                dve.wait_ge(dve_chain, chain[0])

            def power_of_two(dst, src, scale):
                link(nc.vector.tensor_scalar(dst, src, TINY, None, ALU.max))
                link(nc.vector.reciprocal(dst, dst))
                link(nc.vector.tensor_scalar(dst.bitcast(U32), dst.bitcast(U32), EXPONENT, None, ALU.bitwise_and))
                link(nc.vector.tensor_scalar(dst, dst, scale, None, ALU.mult))

            def layernorm_stats(m):
                dve.wait_ge(x_loaded[m], 16)
                for i in range(BATCH):
                    last = nc.vector.bn_stats(stats[:, i, :], res[:, m * BATCH + i, :])
                link(last)
                for i in range(BATCH):
                    last = nc.vector.bn_aggr(mv[:, m * BATCH + i, :], stats[:, i, :])
                last.then_inc(stats_ready, 1)

            def normalise(b):
                if b % BATCH == 0:
                    dve.wait_ge(r_ready, b // BATCH + 1)
                    dve.wait_ge(stats_ready, b // BATCH + 1)
                if b >= 4:
                    dve.wait_ge(xh_ready, b - 3)
                    dve.wait_ge(xl_ready, b - 3)
                nc.vector.tensor_scalar(xn[:, b % 4, :], res[:, b, :], mv[:, b, 0:1], col(r1, b), ALU.subtract, ALU.mult).then_inc(xn_ready, 1)

            def projected(q, b, par):
                dve.wait_ge(proj_mm, NB * q + b + 1)
                nc.vector.scalar_tensor_tensor(
                    out=vx[:, :, :, bass.ds(b, 1)].rearrange("p i c o -> p i (c o)"), in0=bank_c[par][:, 0:3 * CQ].rearrange("p (i c) -> p i c", i=3),
                    scalar=r2[:, bass.ds(b, 1)], in1=bias[:, bass.ds(q * 3 * CQ, 3 * CQ)].rearrange("p (i c) -> p i c", i=3),
                    op0=ALU.mult, op1=ALU.add).then_inc(proj_ev, 1)

            def split_v(q, m):
                dve.wait_ge(vh_ready, NSPLIT * q + m + 1)
                cols = bass.ds(SPLIT * m, SPLIT)
                nc.vector.tensor_tensor(vhl[:, 1, :, cols], vx[:, 0, :, cols], vhl[:, 0, :, cols], ALU.subtract).then_inc(vl_ready, 1)

            layernorm_stats(0)
            nc.vector.memset(ones, 1.0)
            link(nc.vector.memset(kpd[:, :, :, :, :].rearrange("p h v w e -> p (h v w e)").bitcast(F32), 0.0))
            dve.wait_ge(gb_loaded, 16 * 2 * KD)
            dve.wait_ge(win_loaded, 16)
            for k in range(KD):
                nc.vector.tensor_scalar(bbc[:, k, :], ones, gb[:, 1, k:k + 1], None, ALU.mult)
                last = nc.vector.tensor_scalar(wgm[:, k, :], win[:, k, :], gb[:, 0, k:k + 1], None, ALU.mult)
            link(last)
            nc.vector.tensor_tensor(wsq[:, :, :], wgm[:, :, :], wgm[:, :, :], ALU.mult).then_inc(wsq_ready, 1)

            dve.wait_ge(k_loaded, 64)
            link(nc.vector.tensor_reduce(kmax[:, 0, :, :], kin[:, :, :, :], AX.X, ALU.max, apply_absolute_value=True))
            kscale = kmax[:, 1, :, :].rearrange("p h v -> p (h v)")
            power_of_two(kscale, kmax[:, 0, :, :].rearrange("p h v -> p (h v)"), KTOP)
            for h in range(KD):
                for v in range(2):
                    last = nc.vector.tensor_scalar(kin[:, h, v, :], kin[:, h, v, :], kmax[:, 1, h, v:v + 1], None, ALU.mult)
            link(last)
            taps = [kpd[:, :, :, ROWS:ROWS + K, e] for e in range(2)]
            link(nc.vector.tensor_copy(taps[0], kin[:, :, :, :]))
            nc.vector.tensor_tensor(taps[1], kin[:, :, :, :], taps[0], ALU.subtract).then_inc(kpad_ready, 2)

            layernorm_stats(1)

            half = 3 * D // 2
            dve.wait_ge(norm_mm, 1)
            dve.wait_ge(bin_loaded, 16)
            for i in range(2):
                cols = slice(i * half, (i + 1) * half)
                last = nc.vector.tensor_tensor(bin_row[:, cols], bank_u[i][:, 0:half], bin_row[:, cols], ALU.add)
            link(last)
            link(nc.vector.scalar_tensor_tensor(out=scl, in0=bin_row, scalar=-1.0, in1=bin_row, op0=ALU.mult, op1=ALU.max))
            dve.wait_ge(norm_ready, 2)
            link(nc.vector.tensor_tensor(scl, scl, nrm, ALU.add))
            link(nc.vector.tensor_scalar(scl, scl, TINY, None, ALU.max))
            link(nc.vector.tensor_scalar(scl.bitcast(I32), scl.bitcast(I32), EXPONENT, None, ALU.bitwise_and))
            link(nc.vector.tensor_scalar(scl.bitcast(I32), scl.bitcast(I32), -1.0, float(254 << 23), ALU.mult, ALU.add))
            link(nc.vector.tensor_scalar(scl, scl, TOP / 2, None, ALU.mult))
            for k in range(KD):
                nc.vector.tensor_tensor(wgm[:, k, :], wgm[:, k, :], scl, ALU.mult).then_inc(wgm_ready, 1)

            def by_quarter(ap):
                return ap.rearrange("p (i q c) -> p i q c", q=NQ, i=3)

            def in_quarters(ap):
                return ap.rearrange("p (q i c) -> p i q c", q=NQ, i=3)

            link(nc.vector.tensor_tensor(in_quarters(bias[:, :]), by_quarter(bin_row), by_quarter(scl), ALU.mult))
            for b in range(4):
                normalise(b)
            for k in range(KD):
                dve.wait_ge(wqh_ready, k + 1)
                nc.vector.tensor_tensor(in_quarters(wq[:, 1, k, :]), by_quarter(wgm[:, k, :]), in_quarters(wq[:, 0, k, :]), ALU.subtract).then_inc(wql_ready, 1)

            dve.wait_ge(consts_ready, 1)
            for i in range(6):
                link(nc.vector.tensor_tensor(dg[:, 0:P], scl[:, i * P:(i + 1) * P], ident32, ALU.mult))
                link(nc.vector.tensor_reduce(sdg[:, i:i + 1], dg[:, 0:P], AX.X, ALU.add))
            link(nc.vector.tensor_tensor(qch[:, :], sdg[:, 0:2], sdg[:, 2:4], ALU.mult))
            link(nc.vector.tensor_scalar(qch[:, :], qch[:, :], Y1_SCALE, None, ALU.mult))
            link(nc.vector.tensor_tensor(qch[:, :], qch[:, :], sdg[:, 4:6], ALU.mult))
            link(nc.vector.tensor_tensor(qch[:, :], qch[:, :], kmax[:, 1, :, 0], ALU.mult))
            link(nc.vector.tensor_tensor(qch[:, :], qch[:, :], kmax[:, 1, :, 1], ALU.mult))
            link(nc.vector.reciprocal(qch[:, :], qch[:, :]))
            dve.wait_ge(wout_loaded, 16)
            for k in range(KD):
                last = nc.vector.tensor_scalar(wout[:, k, :], wout[:, k, :], col(qch, k), None, ALU.mult)
            link(last)
            nc.vector.tensor_reduce(c(C_OP), wout[:, :, :].rearrange("p k n -> p (k n)"), AX.X, ALU.max, apply_absolute_value=True).then_inc(part_max, 1)

            def unit(u):
                if u < 2 * HB:
                    return gu_int[:, u, :], c(C_SC + u // HB)
                return wd_int[:, (u - 2 * HB) // 3, ((u - 2 * HB) % 3) * D:((u - 2 * HB) % 3 + 1) * D], c(C_SC + 2)

            for b in range(4, NB + 4):
                if b >= BATCH and b % BATCH == 0 and b // BATCH + 1 < NBATCH:
                    layernorm_stats(b // BATCH + 1)
                if b < NB:
                    normalise(b)
                projected(0, b - 4, (b - 4) % 2)
                if (b - 4) % SPLIT == SPLIT - 1 and b - 4 > SPLIT:
                    split_v(0, (b - 4) // SPLIT - 1)
                if b == 11:
                    dve.wait_ge(all_max, 1)
                    power_of_two(c(C_OS), c(C_OM), TOP / 8)
                    for k in range(KD):
                        last = nc.vector.tensor_scalar(wout[:, k, :], wout[:, k, :], c(C_OS), None, ALU.mult)
                    link(last)
                    link(nc.vector.tensor_copy(wo[:, 0, :, :], wout[:, :, :]))
                    nc.vector.tensor_tensor(wo[:, 1, :, :], wout[:, :, :], wo[:, 0, :, :], ALU.subtract).then_inc(wo_ready, 2)
                if b == 15:
                    dve.wait_ge(int_loaded, 48)
                    for i, src in enumerate((gu_int[:, 0:HB, :].rearrange("p u d -> p (u d)"),
                                             gu_int[:, HB:2 * HB, :].rearrange("p u d -> p (u d)"),
                                             wd_int[:, :, :].rearrange("p a h -> p (a h)"))):
                        last = nc.vector.tensor_reduce(c(C_PMAX + i), src, AX.X, ALU.max, apply_absolute_value=True)
                    last.then_inc(part_max, 1)
                if b == 23:
                    dve.wait_ge(all_max, 2)
                    power_of_two(c(C_SC, 3), c(C_MAX, 3), TOP)
                    link(nc.vector.tensor_scalar(c(C_SC, 3), c(C_SC, 3), 1.0, None, ALU.min))
                    link(nc.vector.reciprocal(c(C_REC, 3), c(C_SC, 3)))
                    nc.vector.tensor_scalar(c(C_GS), c(C_REC), 1.0 / 127.0, None, ALU.mult)
                    link(nc.vector.tensor_tensor(c(C_T), c(C_MAX), c(C_MAX + 1), ALU.mult))
                    link(nc.vector.tensor_tensor(c(C_T), c(C_T), c(C_SC + 1), ALU.mult))
                    link(nc.vector.tensor_scalar(c(C_T), c(C_T), XN_MAX ** 4 * D / 127.0 / D * D, None, ALU.mult))
                    power_of_two(c(C_HS), c(C_T), TOP)
                    link(nc.vector.reciprocal(c(C_FS), c(C_HS)))
                    link(nc.vector.tensor_tensor(c(C_FS), c(C_FS), c(C_REC + 1), ALU.mult))
                    link(nc.vector.tensor_tensor(c(C_FS), c(C_FS), c(C_REC + 2), ALU.mult))
                    nc.vector.tensor_scalar(c(C_FS), c(C_FS), 1.0 / 127.0 / 127.0, None, ALU.mult).then_inc(ffn_consts, 1)
            split_v(0, NSPLIT - 1)
            dve.wait_ge(ffn_consts, 1)
            for u in range(3 * HB):
                src, s = unit(u)
                dve.wait_ge(unit_h, u + 1)
                if u >= 4:
                    dve.wait_ge(unit_tp, u - 3)
                nc.vector.scalar_tensor_tensor(out=units[u % 4][:, 1, :], in0=src, scalar=s, in1=units[u % 4][:, 0, :],
                                               op0=ALU.mult, op1=ALU.subtract).then_inc(unit_l, 1)
            dve.wait_ge(unit_ev, 3 * HB)
            link(nc.vector.tensor_reduce(c(C_T), wgu[:, 1, :, :].rearrange("p k n -> p (k n)"), AX.X, ALU.max, apply_absolute_value=True))
            link(nc.vector.tensor_reduce(c(C_T2), wd[:, 1, :, :].rearrange("p k n -> p (k n)"), AX.X, ALU.max, apply_absolute_value=True))
            nc.vector.tensor_tensor(c(C_LP), c(C_T), c(C_T2), ALU.max).then_inc(part_max, 1)
            dve.wait_ge(all_max, 3)
            nc.vector.tensor_scalar(flag[:, :], c(C_OP), 0.0, None, ALU.is_gt).then_inc(flag_ready, 1)

            def hidden(q, j):
                n = SQ * q + j
                dve.wait_ge(sg_ready, n + 1)
                dve.wait_ge(gu_mm, n + 1)
                nc.vector.scalar_tensor_tensor(out=sgh[:, j % 2, :], in0=bank_u[j % 2][:, :], scalar=c(C_HS), in1=sgh[:, j % 2, :],
                                               op0=ALU.mult, op1=ALU.mult).then_inc(h_ready, 1)

            def split_h(q, j, first):
                n = SQ * q + j
                dve.wait_ge(hh_ready, n + 1)
                nc.vector.tensor_tensor(hhl[:, j % 3, 1, :], sgh[:, j % 2, :], hhl[:, j % 3, 0, :], ALU.subtract).then_inc(hl_ready, 1)

            def fold(q, chunk_of_q, first=False):
                chunk = 2 * q + chunk_of_q
                dve.wait_ge(down_mm, HB * (chunk + 1))
                if first:
                    dve.wait_ge(bout_added, NB)
                for a in range(2):
                    tiles = res[:, bass.ds(TPC * chunk + 2 * a, 2), :].rearrange("p b d -> p (b d)")
                    nc.vector.scalar_tensor_tensor(out=tiles, in0=bank_d[a][:, :], scalar=c(C_FS), in1=tiles,
                                                   op0=ALU.mult, op1=ALU.add).then_inc(folded, 1)

            def gate_1(q, g):
                G = GQ * q + g
                dve.wait_ge(conv_mm, 2 * G + 1)
                nc.vector.scalar_tensor_tensor(out=y1f[:, :, :].rearrange("p c b -> p (c b)"), in0=bank_c[0][:, :], scalar=Y1_SCALE,
                                               in1=vx[:, 1, g * CG:(g + 1) * CG, :].rearrange("p c b -> p (c b)"),
                                               op0=ALU.mult, op1=ALU.mult).then_inc(y1_ready, 1)

            def split_y1(q, g):
                dve.wait_ge(y1h_ready, GQ * q + g + 1)
                nc.vector.tensor_tensor(y1hl[:, 1, :, :], y1f[:, :, :], y1hl[:, 0, :, :], ALU.subtract).then_inc(y1l_ready, 1)

            def gate_2(q, g):
                G = GQ * q + g
                dve.wait_ge(conv_mm, 2 * G + 2)
                nc.vector.tensor_tensor(y2[:, bass.ds(CG * G, CG), :].rearrange("p c b -> p (c b)"), bank_c[1][:, :],
                                        vx[:, 2, g * CG:(g + 1) * CG, :].rearrange("p c b -> p (c b)"), ALU.mult).then_inc(y2_ready, 1)

            def token_max(q, g):
                G = GQ * q + g
                dve.wait_ge(y2_ready, G + 1)
                nc.vector.tensor_reduce(ymax[:, bass.ds(G, 1), :].rearrange("p g b -> p (g b)"),
                                        y2[:, bass.ds(CG * G, CG), :].rearrange("p c b -> p b c"),
                                        AX.X, ALU.max, apply_absolute_value=True).then_inc(ymax_ready, 1)

            def ffn_step(q, j, first, between=None):
                hidden(q, j)
                if between is not None:
                    between()
                if not (first and j < 1):
                    split_h(q - 1 if j < 1 else q, (j - 1) % SQ, first)
                if j % HB == 1 and not (first and j < HB):
                    fold(q - 1 if j < 2 else q, 1 if j < 2 else 0, first)

            def quarter(q, first):
                if not first:
                    for i in range(SPLIT):
                        projected(q, i, i % 2)
                    with dve.Fori(1, NSPLIT) as m:
                        for i in range(SPLIT):
                            projected(q, SPLIT * m + i, i % 2)
                        split_v(q, m - 1)
                    split_v(q, NSPLIT - 1)
                for g in range(GQ):
                    ffn_step(q, SG * g, first, (lambda: token_max(q, g - 1)) if g > 0 else None)
                    gate_1(q, g)
                    ffn_step(q, SG * g + 1, first, lambda: split_y1(q, g))
                    ffn_step(q, SG * g + 2, first)
                    gate_2(q, g)
                token_max(q, GQ - 1)

            quarter(0, True)
            with dve.Fori(1, NQ) as q:
                quarter(q, False)

            dve.wait_ge(ymax_ready, NG)
            link(nc.vector.tensor_reduce(st[:, 2, :], ymax[:, :, :].rearrange("p g b -> p b g"), AX.X, ALU.max))
            power_of_two(st[:, 0, :], st[:, 2, :], TOP)
            link(nc.vector.tensor_scalar(st[:, 1, :], st[:, 0, :], c(C_OS), None, ALU.mult))
            link(nc.vector.reciprocal(st[:, 1, :], st[:, 1, :]))

            def scale_y(b, r, first):
                if not first:
                    dve.wait_ge(yh_ready, b - 3)
                    dve.wait_ge(yl_ready, b - 3)
                nc.vector.tensor_scalar(ysc[:, r, :], y2[:, :, bass.ds(b, 1)].rearrange("p c o -> p (c o)"), st[:, 0, bass.ds(b, 1)], None,
                                        ALU.mult).then_inc(ysc_ready, 1)

            def finish(b, par):
                dve.wait_ge(out_mm, b + 1)
                o = res[:, bass.ds(b, 1), :].rearrange("p o d -> p (o d)")
                nc.vector.scalar_tensor_tensor(out=o, in0=bank_c[par][:, 0:D], scalar=st[:, 1, bass.ds(b, 1)], in1=o,
                                               op0=ALU.mult, op1=ALU.add).then_inc(out_ready, 1)

            for r in range(4):
                scale_y(r, r, True)
            split_h(NQ - 1, SQ - 1, False)
            fold(NQ - 1, 1)
            dve.wait_ge(folded, 2 * NCHUNK)
            with dve.Fori(1, NB // 4) as i:
                for r in range(4):
                    scale_y(4 * i + r, r, False)
                    finish(4 * i + r - 4, r % 2)
            for r in range(4):
                finish(NB - 4 + r, r % 2)

        @block.gpsimd
        def _(pool):
            chain = [0]

            def link(ins):
                chain[0] += 1
                ins.then_inc(pool_chain, 1)
                pool.wait_ge(pool_chain, chain[0])

            nc.gpsimd.memset(minus_half[:, :], -0.5)
            link(nc.gpsimd.memset(ident32, 0.0))
            link(nc.gpsimd.affine_select(out=ident32, in_=ident32, compare_op=ALU.not_equal, fill=1.0, base=0,
                                         pattern=[[-1, P]], channel_multiplier=1))
            nc.gpsimd.tensor_copy(ident[:, :], ident32).then_inc(consts_ready, 1)

            def layernorm_scales(m):
                pool.wait_ge(stats_ready, m + 1)
                s = slice(m * BATCH, (m + 1) * BATCH)
                mean, var = mv[:, s, 0], mv[:, s, 1]
                link(nc.gpsimd.tensor_scalar(ls0[:, s], var, EPS, None, ALU.add))
                link(nc.gpsimd.tensor_tensor(r1[:, s], ls0[:, s], minus_half[:, :], ALU.pow))
                nc.gpsimd.tensor_scalar(r1p[:, s], r1[:, s], 1.0, None, ALU.add)
                link(nc.gpsimd.tensor_tensor(ls1[:, s], mean, r1[:, s], ALU.mult))
                nc.gpsimd.tensor_scalar(nmr[:, s], ls1[:, s], -1.0, None, ALU.mult).then_inc(r_ready, 1)
                link(nc.gpsimd.tensor_tensor(ls0[:, s], var, r1[:, s], ALU.mult))
                link(nc.gpsimd.tensor_tensor(ls0[:, s], ls0[:, s], r1[:, s], ALU.mult))
                link(nc.gpsimd.tensor_scalar(ls0[:, s], ls0[:, s], EPS, None, ALU.add))
                link(nc.gpsimd.tensor_tensor(r2[:, s], ls0[:, s], minus_half[:, :], ALU.pow))

            def split_x(b):
                pool.wait_ge(xn_ready, b + 1)
                pool.wait_ge(xh_ready, b + 1)
                nc.gpsimd.tensor_tensor(xhl[:, 2 * (b % 4) + 1, :], xn[:, b % 4, :], xhl[:, 2 * (b % 4), :], ALU.subtract).then_inc(xl_ready, 1)

            def reduce_max(dst, src, n):
                pool.wait_ge(part_max, n)
                nc.gpsimd.partition_all_reduce(dst, src, P, bass.bass_isa.ReduceOp.max).then_inc(all_max, 1)

            layernorm_scales(0)
            nc.gpsimd.memset(bands[:, :, :, :, :].rearrange("p v c w e -> p (v c w e)").bitcast(F32), 0.0).then_inc(bands_zeroed, 1)
            layernorm_scales(1)
            for b in range(NB):
                if b >= BATCH and b % BATCH == 2 and b // BATCH + 1 < NBATCH:
                    layernorm_scales(b // BATCH + 1)
                split_x(b)
                if b == 6:
                    reduce_max(c(C_OM), c(C_OP), 1)
                if b == 14:
                    reduce_max(c(C_MAX, 3), c(C_PMAX, 3), 2)
            def add_xn(b):
                pool.wait_ge(r_ready, b // BATCH + 1)
                nc.gpsimd.tensor_scalar(res[:, b, :], res[:, b, :], col(r1p, b), col(nmr, b), ALU.mult, ALU.add).then_inc(res_ready, 1)

            pool.wait_ge(bout_loaded, 16)
            for b in range(NB):
                if b == 0:
                    add_xn(0)
                if b + 1 < NB:
                    add_xn(b + 1)
                if b == 12:
                    reduce_max(c(C_OP), c(C_LP), 3)
                pool.wait_ge(res_ready, b + 1)
                nc.gpsimd.tensor_tensor(res[:, b, :], res[:, b, :], bout[:, :], ALU.add).then_inc(bout_added, 1)
            def split_y(b, r, first):
                pool.wait_ge(ysc_ready, b + 1)
                pool.wait_ge(yh_ready, b + 1)
                nc.gpsimd.tensor_tensor(yhl[:, r, 1, :], ysc[:, r, :], yhl[:, r, 0, :], ALU.subtract).then_inc(yl_ready, 1)

            with pool.Fori(0, NB // 4) as i:
                for r in range(4):
                    split_y(4 * i + r, r, False)


_INS = ["L0_attn_x", "L0_attn_W_in", "L0_attn_b_in", "L0_attn_k0", "L0_attn_k1", "L0_attn_gamma", "L0_attn_beta",
        "L0_attn_W_out", "L0_attn_b_out", "L0_ffn_w_gate", "L0_ffn_w_up", "L0_ffn_w_down"]


def kernel(**inputs):
    import numpy as np
    import concourse.bacc as bacc
    from concourse.bass_utils import run_bass_kernel_spmd

    nc = bacc.Bacc("TRN2", target_bir_lowering=False, num_devices=1)
    arrays, args = {}, []
    for name in _INS:
        a = np.ascontiguousarray(inputs[name])
        arrays[f"in_{name}"] = a
        args.append(nc.dram_tensor(f"in_{name}", a.shape, mybir.dt.from_np(a.dtype), kind="ExternalInput").ap())
    out = nc.dram_tensor("out_0", arrays["in_L0_attn_x"].shape, F32, kind="ExternalOutput").ap()
    hyena_ffn_kernel(nc, *args, out)
    r = run_bass_kernel_spmd(nc, [arrays], core_ids=[0])
    return r.results[0]["out_0"]
```
